# Optimizing a Trainium2 kernel written in Bass

```python
import numpy as np
import jax
import jax.numpy as jnp

def _softmax(x, axis=-1):
    return jax.nn.softmax(x, axis=axis)

def _gelu(x):
    return jax.nn.gelu(x, approximate=True)

def _silu(x):
    return jax.nn.silu(x)

def _sigmoid(x):
    return jax.nn.sigmoid(x)

def _layernorm(x, axis=-1, eps=1e-05):
    m = jnp.mean(x, axis=axis, keepdims=True)
    v = jnp.var(x, axis=axis, keepdims=True)
    return (x - m) / jnp.sqrt(v + eps)

def _scatter_add(tgt, idx, src, axis=0):
    return tgt.at[idx].add(src)

def _segment_sum(src, seg, n):
    return jax.ops.segment_sum(src, seg, n)
kernel_name = 'mk_dlrm_tower_d1_rec_r8_cc8c44'

def setup_inputs(seed: int=0):
    np.random.seed(seed)
    _w = jnp.asarray

    def _rec_inputs():
        import jax
        import jax.numpy as jnp
        _tk = jax.random.key(seed)
        dense_ctx = jax.random.normal(jax.random.fold_in(_tk, 190), (512, 16), jnp.float32)
        ids = jnp.stack([jax.random.randint(jax.random.fold_in(_tk, 200 + f), (512,), 0, v, jnp.int32) for f, v in enumerate([125000, 12500, 12500, 1250, 1000, 1250, 1000, 1000, 1000, 1250, 1250, 1000, 1000, 1250, 1250, 1000, 1250, 12500, 1250, 1250, 1000, 1000, 1250, 12500, 12500, 12500, 12500])], axis=1)
        tbl_0 = 0.05 * jax.random.normal(jax.random.fold_in(_tk, 500 + 0), (125000, 128), jnp.float32)
        tbl_1 = 0.05 * jax.random.normal(jax.random.fold_in(_tk, 500 + 1), (12500, 128), jnp.float32)
        tbl_2 = 0.05 * jax.random.normal(jax.random.fold_in(_tk, 500 + 2), (12500, 128), jnp.float32)
        tbl_3 = 0.05 * jax.random.normal(jax.random.fold_in(_tk, 500 + 3), (1250, 128), jnp.float32)
        tbl_4 = 0.05 * jax.random.normal(jax.random.fold_in(_tk, 500 + 4), (1000, 128), jnp.float32)
        tbl_5 = 0.05 * jax.random.normal(jax.random.fold_in(_tk, 500 + 5), (1250, 128), jnp.float32)
        tbl_6 = 0.05 * jax.random.normal(jax.random.fold_in(_tk, 500 + 6), (1000, 128), jnp.float32)
        tbl_7 = 0.05 * jax.random.normal(jax.random.fold_in(_tk, 500 + 7), (1000, 128), jnp.float32)
        tbl_8 = 0.05 * jax.random.normal(jax.random.fold_in(_tk, 500 + 8), (1000, 128), jnp.float32)
        tbl_9 = 0.05 * jax.random.normal(jax.random.fold_in(_tk, 500 + 9), (1250, 128), jnp.float32)
        tbl_10 = 0.05 * jax.random.normal(jax.random.fold_in(_tk, 500 + 10), (1250, 128), jnp.float32)
        tbl_11 = 0.05 * jax.random.normal(jax.random.fold_in(_tk, 500 + 11), (1000, 128), jnp.float32)
        tbl_12 = 0.05 * jax.random.normal(jax.random.fold_in(_tk, 500 + 12), (1000, 128), jnp.float32)
        tbl_13 = 0.05 * jax.random.normal(jax.random.fold_in(_tk, 500 + 13), (1250, 128), jnp.float32)
        tbl_14 = 0.05 * jax.random.normal(jax.random.fold_in(_tk, 500 + 14), (1250, 128), jnp.float32)
        tbl_15 = 0.05 * jax.random.normal(jax.random.fold_in(_tk, 500 + 15), (1000, 128), jnp.float32)
        tbl_16 = 0.05 * jax.random.normal(jax.random.fold_in(_tk, 500 + 16), (1250, 128), jnp.float32)
        tbl_17 = 0.05 * jax.random.normal(jax.random.fold_in(_tk, 500 + 17), (12500, 128), jnp.float32)
        tbl_18 = 0.05 * jax.random.normal(jax.random.fold_in(_tk, 500 + 18), (1250, 128), jnp.float32)
        tbl_19 = 0.05 * jax.random.normal(jax.random.fold_in(_tk, 500 + 19), (1250, 128), jnp.float32)
        tbl_20 = 0.05 * jax.random.normal(jax.random.fold_in(_tk, 500 + 20), (1000, 128), jnp.float32)
        tbl_21 = 0.05 * jax.random.normal(jax.random.fold_in(_tk, 500 + 21), (1000, 128), jnp.float32)
        tbl_22 = 0.05 * jax.random.normal(jax.random.fold_in(_tk, 500 + 22), (1250, 128), jnp.float32)
        tbl_23 = 0.05 * jax.random.normal(jax.random.fold_in(_tk, 500 + 23), (12500, 128), jnp.float32)
        tbl_24 = 0.05 * jax.random.normal(jax.random.fold_in(_tk, 500 + 24), (12500, 128), jnp.float32)
        tbl_25 = 0.05 * jax.random.normal(jax.random.fold_in(_tk, 500 + 25), (12500, 128), jnp.float32)
        tbl_26 = 0.05 * jax.random.normal(jax.random.fold_in(_tk, 500 + 26), (12500, 128), jnp.float32)
        _rk = jax.random.fold_in(_tk, 7)
        W_top1 = 0.0521996 * jax.random.normal(jax.random.fold_in(_tk, 801), (367, 512), jnp.float32)
        W_top2 = 0.0441942 * jax.random.normal(jax.random.fold_in(_tk, 802), (512, 256), jnp.float32)
        W_top3 = 0.0625 * jax.random.normal(jax.random.fold_in(_tk, 803), (256, 1), jnp.float32)
        b_top1 = jnp.zeros((512,), jnp.float32)
        b_top2 = jnp.zeros((256,), jnp.float32)
        return (dense_ctx, ids, tbl_0, tbl_1, tbl_2, tbl_3, tbl_4, tbl_5, tbl_6, tbl_7, tbl_8, tbl_9, tbl_10, tbl_11, tbl_12, tbl_13, tbl_14, tbl_15, tbl_16, tbl_17, tbl_18, tbl_19, tbl_20, tbl_21, tbl_22, tbl_23, tbl_24, tbl_25, tbl_26, W_top1, b_top1, W_top2, b_top2, W_top3)
    dense_ctx, ids, tbl_0, tbl_1, tbl_2, tbl_3, tbl_4, tbl_5, tbl_6, tbl_7, tbl_8, tbl_9, tbl_10, tbl_11, tbl_12, tbl_13, tbl_14, tbl_15, tbl_16, tbl_17, tbl_18, tbl_19, tbl_20, tbl_21, tbl_22, tbl_23, tbl_24, tbl_25, tbl_26, W_top1, b_top1, W_top2, b_top2, W_top3 = _rec_inputs()

    def _L0_rec_setup():
        import jax, jax.numpy as jnp
        import numpy as np

        def _tri_indices(num_feas):
            return np.array([i * num_feas + j for j in range(1, num_feas) for i in range(j)], dtype=np.int32)
        key = jax.random.key(seed)
        batch, num_feas, embed_dim = (2048, 27, 128)
        inputs = jax.random.normal(key, (batch, num_feas, embed_dim), dtype=jnp.float32)
        return {'inputs': inputs, 'num_feas': num_feas}
    _L0_rec_all = _L0_rec_setup()
    _L0_rec_in = {k: v for k, v in _L0_rec_all.items() if k in ()}
    del _L0_rec_all
    return {'dense_ctx': dense_ctx, 'ids': ids, 'tbl_0': tbl_0, 'tbl_1': tbl_1, 'tbl_2': tbl_2, 'tbl_3': tbl_3, 'tbl_4': tbl_4, 'tbl_5': tbl_5, 'tbl_6': tbl_6, 'tbl_7': tbl_7, 'tbl_8': tbl_8, 'tbl_9': tbl_9, 'tbl_10': tbl_10, 'tbl_11': tbl_11, 'tbl_12': tbl_12, 'tbl_13': tbl_13, 'tbl_14': tbl_14, 'tbl_15': tbl_15, 'tbl_16': tbl_16, 'tbl_17': tbl_17, 'tbl_18': tbl_18, 'tbl_19': tbl_19, 'tbl_20': tbl_20, 'tbl_21': tbl_21, 'tbl_22': tbl_22, 'tbl_23': tbl_23, 'tbl_24': tbl_24, 'tbl_25': tbl_25, 'tbl_26': tbl_26, 'W_top1': W_top1, 'b_top1': b_top1, 'W_top2': W_top2, 'b_top2': b_top2, 'W_top3': W_top3}

def reference(dense_ctx, ids, tbl_0, tbl_1, tbl_2, tbl_3, tbl_4, tbl_5, tbl_6, tbl_7, tbl_8, tbl_9, tbl_10, tbl_11, tbl_12, tbl_13, tbl_14, tbl_15, tbl_16, tbl_17, tbl_18, tbl_19, tbl_20, tbl_21, tbl_22, tbl_23, tbl_24, tbl_25, tbl_26, W_top1, b_top1, W_top2, b_top2, W_top3):
    import jax
    import jax.numpy as jnp

    def _L0_rec_ref(inputs, num_feas):
        import jax, jax.numpy as jnp
        import numpy as np

        def _tri_indices(num_feas):
            return np.array([i * num_feas + j for j in range(1, num_feas) for i in range(j)], dtype=np.int32)
        dot = jnp.einsum('bnd,bmd->bnm', inputs, inputs)
        idx = jnp.asarray(_tri_indices(num_feas))
        flat = dot.reshape(inputs.shape[0], num_feas * num_feas)
        return flat[:, idx]
    e = jnp.stack([tbl_0[ids[:, 0]], tbl_1[ids[:, 1]], tbl_2[ids[:, 2]], tbl_3[ids[:, 3]], tbl_4[ids[:, 4]], tbl_5[ids[:, 5]], tbl_6[ids[:, 6]], tbl_7[ids[:, 7]], tbl_8[ids[:, 8]], tbl_9[ids[:, 9]], tbl_10[ids[:, 10]], tbl_11[ids[:, 11]], tbl_12[ids[:, 12]], tbl_13[ids[:, 13]], tbl_14[ids[:, 14]], tbl_15[ids[:, 15]], tbl_16[ids[:, 16]], tbl_17[ids[:, 17]], tbl_18[ids[:, 18]], tbl_19[ids[:, 19]], tbl_20[ids[:, 20]], tbl_21[ids[:, 21]], tbl_22[ids[:, 22]], tbl_23[ids[:, 23]], tbl_24[ids[:, 24]], tbl_25[ids[:, 25]], tbl_26[ids[:, 26]]], axis=1)
    z = _L0_rec_ref(e, 27)
    z = z.reshape(z.shape[0], -1)
    h = jnp.concatenate([z, dense_ctx], axis=1)
    h = jnp.maximum(h @ W_top1 + b_top1, 0.0)
    h = jnp.maximum(h @ W_top2 + b_top2, 0.0)
    y = h @ W_top3
    return y

_drawn_inputs = setup_inputs


def setup_inputs(seed=0):
    import zlib

    import numpy as np

    out = dict(_drawn_inputs(seed))
    spreads = {'b_top1': (0.0, 0.1), 'b_top2': (0.0, 0.1)}
    factors = {}
    for name, (base, spread) in spreads.items():
        noise = np.random.default_rng([zlib.crc32(name.encode()), seed]).standard_normal(out[name].shape)
        drawn = base * np.exp(spread * noise) if base else spread * noise
        out[name] = jnp.asarray(drawn.astype(out[name].dtype))
    for name, factor in factors.items():
        out[name] = (out[name] * factor).astype(out[name].dtype)
    return out
```

```python
from contextlib import ExitStack

import concourse.bass as bass
from concourse import mybir

F32 = mybir.dt.float32
I32 = mybir.dt.int32
ALU = mybir.AluOpType
ACT = mybir.ActivationFunctionType

P = 128
QUAD = 32
QUADS = P // QUAD


def build_tower(nc, ids, dense_ctx_t, tables, W1, b1, W2, b2, W3, out):
    batch, FEATS = ids.shape
    D = tables[0].shape[1]
    TILES = batch // P
    CTX = dense_ctx_t.shape[0]
    H1, H2 = W2.shape
    H1C, H2C = H1 // P, H2 // P
    COLS = FEATS - 1
    SLOTS = -(-COLS // QUADS)
    LAST_Q = COLS - QUADS * (SLOTS - 1)
    K_LAST = QUAD * LAST_Q + CTX
    BANKF = 4
    FGROUPS = [list(range(f, min(f + BANKF, FEATS))) for f in range(0, FEATS, BANKF)]
    NFG = len(FGROUPS)
    SG, GB, UB = QUADS, 4, 2
    UNITG = GB * UB
    UNITS = P // (SG * UNITG)

    with ExitStack() as ctx:
        def sb(name, shape, dt=F32):
            return ctx.enter_context(nc.sbuf_tensor(name, shape, dt))

        def pb(name, shape):
            return ctx.enter_context(nc.psum_tensor(name, shape, F32))

        def sem(name):
            return ctx.enter_context(nc.semaphore(name))

        ids_sb = sb("ids_sb", [P, TILES, FEATS], I32)
        emb = sb("emb", [P, FEATS, D])
        embT = sb("embT", [P, P, QUAD])
        pairs = sb("pairs", [P, TILES, SLOTS, P])
        w1_sb = sb("w1_sb", [P, SLOTS, H1])
        w2_sb = sb("w2_sb", [P, H1C, H2])
        w3_sb = sb("w3_sb", [P, H2C])
        b1_sb = sb("b1_sb", [P, H1C])
        b2_sb = sb("b2_sb", [P, H2C])
        h1T = sb("h1T", [P, H1C, P])
        h2T = sb("h2T", [P, H2C, P])
        y_sb = sb("y_sb", [P, TILES])
        ident = sb("ident", [P, P])

        tr_ps = pb("tr_ps", [P, 2, BANKF, P])
        gram_ps = pb("gram_ps", [P, 2, UNITG, P])
        mlp_a = pb("mlp_a", [P, 4, P])
        mlp_b = pb("mlp_b", [P, 4, P])

        ids_loaded = sem("ids_loaded")
        gathered = [sem(f"gathered{g}") for g in range(NFG)]
        zeroed = sem("zeroed")
        ident_zero = sem("ident_zero")
        ident_ready = sem("ident_ready")
        w1_loaded = sem("w1_loaded")
        ctx_loaded = sem("ctx_loaded")
        rest_loaded = sem("rest_loaded")
        transposed = sem("transposed")
        embT_by_dve = sem("embT_by_dve")
        embT_by_act = sem("embT_by_act")
        gram_done = sem("gram_done")
        pairs_by_dve = sem("pairs_by_dve")
        pairs_by_act = sem("pairs_by_act")
        h1_done = sem("h1_done")
        relu1_by_act = sem("relu1_by_act")
        relu1_by_dve = sem("relu1_by_dve")
        h2_done = sem("h2_done")
        relu2_done = sem("relu2_done")
        y_done = sem("y_done")
        y_copied = sem("y_copied")
        stored = sem("stored")

        DVE_FG = [g for g in range(NFG) if g % 2 == 0]
        ACT_FG = [g for g in range(NFG) if g % 2 == 1]
        NDVE, NACT = len(DVE_FG), len(ACT_FG)

        block = ctx.enter_context(nc.Block())

        @block.sync
        def _(sp):
            sp.dma_start(ids_sb[:, :, :], ids.rearrange("(p t) f -> p t f", t=TILES)).then_inc(ids_loaded, 16)
            sp.dma_start(b1_sb[:, :], b1).then_inc(rest_loaded, 16)
            sp.dma_start(b2_sb[:, :], b2).then_inc(rest_loaded, 16)
            sp.dma_start(w3_sb[:, :], W3).then_inc(rest_loaded, 16)
            sp.dma_start(w2_sb[:, :, :], W2.rearrange("(c k) n -> k c n", k=P)).then_inc(rest_loaded, 16)
            sp.wait_ge(zeroed, 1)
            row = 0
            for j in range(1, FEATS):
                a, q = divmod(j - 1, QUADS)
                sp.dma_start(w1_sb[QUAD * q:QUAD * q + j, a, :], W1[row:row + j, :]).then_inc(w1_loaded, 16)
                row += j
            sp.dma_start(w1_sb[QUAD * LAST_Q:K_LAST, SLOTS - 1, :], W1[row:row + CTX, :]).then_inc(w1_loaded, 16)
            sp.dma_start(pairs[QUAD * LAST_Q:K_LAST, :, SLOTS - 1, :], dense_ctx_t).then_inc(ctx_loaded, 16)
            sp.wait_ge(y_copied, 1)
            sp.dma_start(out.rearrange("(p t) o -> p (t o)", t=TILES), y_sb[:, :]).then_inc(stored, 16)
            sp.wait_ge(stored, 16)

        @block.gpsimd
        def _(pool):
            nc.gpsimd.memset(ident[:, :], 0.0).then_inc(ident_zero, 1)
            pool.wait_ge(ident_zero, 1)
            nc.gpsimd.affine_select(out=ident[:, :], in_=ident[:, :], compare_op=ALU.not_equal, fill=1.0,
                                    base=0, pattern=[[-1, P]], channel_multiplier=1).then_inc(ident_ready, 1)
            pool.wait_ge(ids_loaded, 16)
            for t in range(TILES):
                for g, group in enumerate(FGROUPS):
                    if t > 0:
                        pool.wait_ge(transposed, NFG * (t - 1) + g + 1)
                    for f in group:
                        pool.indirect_dma_start(emb[:, f, :], None, tables[f],
                                                bass.IndirectOffsetOnAxis(ids_sb[:, t, f:f + 1], 0),
                                                ).then_inc(gathered[g], 16)

        @block.tensor
        def _(pe):
            pe.wait_ge(ident_ready, 1)
            with pe.Fori(0, TILES) as t:
                for g, group in enumerate(FGROUPS):
                    pe.wait_ge(gathered[g], t * (16 * len(group)) + 16 * len(group))
                    if g >= 2:
                        if g % 2 == 0:
                            pe.wait_ge(embT_by_dve, t * NDVE + g // 2)
                        else:
                            pe.wait_ge(embT_by_act, t * NACT + g // 2)
                    for k, f in enumerate(group):
                        last = nc.tensor.transpose(tr_ps[:, g % 2, k, :], emb[:, f, :], ident[:, :])
                    last.then_inc(transposed, 1)
                pe.wait_ge(embT_by_dve, t * NDVE + NDVE)
                pe.wait_ge(embT_by_act, t * NACT + NACT)
                for u in range(UNITS):
                    if u >= 2:
                        pe.wait_ge(pairs_by_dve, t * UNITS + (u - 1))
                        pe.wait_ge(pairs_by_act, t * UNITS + (u - 1))
                    for g in range(UNITG):
                        p0 = SG * (UNITG * u + g)
                        last = nc.tensor.matmul(gram_ps[:, u % 2, g, 0:SG * COLS],
                                                embT[:, p0:p0 + SG, :],
                                                embT[:, p0:p0 + SG, 1:FEATS], start=True, stop=True)
                    last.then_inc(gram_done, 1)
                pe.wait_ge(pairs_by_dve, t * UNITS + UNITS)
                pe.wait_ge(pairs_by_act, t * UNITS + UNITS)
                pe.wait_ge(w1_loaded, 16 * (COLS + 1))
                pe.wait_ge(ctx_loaded, 16)
                for n in range(H1C):
                    bank = mlp_a if n < 2 else mlp_b
                    for a in range(SLOTS):
                        K = P if a < SLOTS - 1 else K_LAST
                        last = nc.tensor.matmul(bank[:, n % 2, :], w1_sb[0:K, a, P * n:P * (n + 1)],
                                                pairs[0:K, bass.ds(t, 1), a, :],
                                                start=(a == 0), stop=(a == SLOTS - 1))
                    if n % 2 == 1:
                        last.then_inc(h1_done, 1)
                pe.wait_ge(rest_loaded, 16 * 4)
                pe.wait_ge(relu1_by_act, t + 1)
                pe.wait_ge(relu1_by_dve, t + 1)
                for m in range(H2C):
                    for c in range(H1C):
                        last = nc.tensor.matmul(mlp_a[:, m, :], w2_sb[:, c, P * m:P * (m + 1)], h1T[:, c, :],
                                                start=(c == 0), stop=(c == H1C - 1))
                last.then_inc(h2_done, 1)
                pe.wait_ge(relu2_done, t + 1)
                for m in range(H2C):
                    last = nc.tensor.matmul(mlp_b[:, 2, bass.ds(t, 1)], h2T[:, m, :], w3_sb[:, m:m + 1],
                                            start=(m == 0), stop=(m == H2C - 1))
                last.then_inc(y_done, 1)

        def move_pairs(copy, u, s, t):
            for q in range(QUADS):
                slots = SLOTS if q < LAST_Q else SLOTS - 1
                src = gram_ps[QUAD * s:QUAD * (s + 1), u % 2, :, COLS * s + q:COLS * s + q + QUADS * (slots - 1) + 1:QUADS]
                p0 = SG * UNITG * u
                dst = pairs[QUAD * q:QUAD * (q + 1), bass.ds(t, 1), 0:slots, p0 + s:p0 + SG * UNITG:SG]
                last = copy(dst.rearrange("r o a g -> r (o g) a"), src)
            return last

        def move_embT(copy, g):
            group = FGROUPS[g]
            return copy(embT[:, :, group[0]:group[-1] + 1],
                        tr_ps[:, g % 2, 0:len(group), :].rearrange("d f p -> d p f"))

        @block.vector
        def _(dve):
            nc.vector.memset(w1_sb[:, :, :], 0.0).then_inc(zeroed, 1)
            nc.vector.memset(embT[:, :, FEATS:QUAD], 0.0)
            with dve.Fori(0, TILES) as t:
                for g in DVE_FG:
                    dve.wait_ge(transposed, t * NFG + (g + 1))
                    move_embT(nc.vector.tensor_copy, g).then_inc(embT_by_dve, 1)
                for u in range(UNITS):
                    dve.wait_ge(gram_done, t * UNITS + (u + 1))
                    for s in (0, 1):
                        last = move_pairs(nc.vector.tensor_copy, u, s, t)
                    last.then_inc(pairs_by_dve, 1)
                dve.wait_ge(h1_done, t * 2 + 2)
                for n in (2, 3):
                    last = nc.vector.tensor_scalar(h1T[:, n, :], mlp_b[:, n % 2, :], b1_sb[:, n:n + 1], 0.0,
                                                   ALU.add, ALU.max)
                last.then_inc(relu1_by_dve, 1)
            dve.wait_ge(y_done, TILES)
            nc.vector.tensor_copy(y_sb[:, :], mlp_b[:, 2, 0:TILES]).then_inc(y_copied, 1)

        @block.scalar
        def _(act):
            act.wait_ge(rest_loaded, 16 * 4)
            with act.Fori(0, TILES) as t:
                for g in ACT_FG:
                    act.wait_ge(transposed, t * NFG + (g + 1))
                    move_embT(nc.scalar.copy, g).then_inc(embT_by_act, 1)
                for u in range(UNITS):
                    act.wait_ge(gram_done, t * UNITS + (u + 1))
                    for s in (2, 3):
                        last = move_pairs(nc.scalar.copy, u, s, t)
                    last.then_inc(pairs_by_act, 1)
                act.wait_ge(h1_done, t * 2 + 1)
                for n in (0, 1):
                    last = nc.scalar.activation(h1T[:, n, :], mlp_a[:, n % 2, :], ACT.Relu, bias=b1_sb[:, n:n + 1])
                last.then_inc(relu1_by_act, 1)
                act.wait_ge(h2_done, t + 1)
                for m in range(H2C):
                    last = nc.scalar.activation(h2T[:, m, :], mlp_a[:, m, :], ACT.Relu, bias=b2_sb[:, m:m + 1])
                last.then_inc(relu2_done, 1)


def kernel(**inputs):
    import numpy as np
    import concourse.bacc as bacc
    from concourse.bass_utils import run_bass_kernel_spmd

    tiles = inputs["ids"].shape[0] // P
    ctx = inputs["dense_ctx"]
    feats = inputs["ids"].shape[1]
    laid = {
        "ids": inputs["ids"],
        "ctx_t": ctx.reshape(P, tiles, ctx.shape[1]).transpose(2, 1, 0),
        "W1": inputs["W_top1"],
        "b1": inputs["b_top1"].reshape(-1, P).T,
        "W2": inputs["W_top2"],
        "b2": inputs["b_top2"].reshape(-1, P).T,
        "W3": inputs["W_top3"].reshape(-1, P).T,
    }
    for f in range(feats):
        laid[f"tbl_{f}"] = inputs[f"tbl_{f}"]

    nc = bacc.Bacc("TRN2", target_bir_lowering=False, num_devices=1)
    arrays, aps = {}, {}
    for name, a in laid.items():
        a = np.ascontiguousarray(a)
        arrays[f"in_{name}"] = a
        aps[name] = nc.dram_tensor(f"in_{name}", a.shape, mybir.dt.from_np(a.dtype), kind="ExternalInput").ap()
    out = nc.dram_tensor("out_y", (inputs["ids"].shape[0], 1), F32, kind="ExternalOutput").ap()
    build_tower(nc, aps["ids"], aps["ctx_t"], [aps[f"tbl_{f}"] for f in range(feats)],
                aps["W1"], aps["b1"], aps["W2"], aps["b2"], aps["W3"], out)
    r = run_bass_kernel_spmd(nc, [arrays], core_ids=[0])
    return r.results[0]["out_y"]
```

```python
from contextlib import ExitStack

import concourse.bass as bass
from concourse import mybir

F32 = mybir.dt.float32
F32R = mybir.dt.float32r
I32 = mybir.dt.int32
ALU = mybir.AluOpType
ACT = mybir.ActivationFunctionType

P = 128
QUAD = 32
QUADS = P // QUAD
LOOKED_UP = [4, 6, 7, 8, 11, 12, 15, 20, 21]
ROWS_K = 125


def runs(features):
    out = []
    for n, f in enumerate(features):
        if out and out[-1][1] + out[-1][2] == f:
            out[-1][2] += 1
        else:
            out.append([n, f, 1])
    return out


def build_tower(nc, ids, ids_by_feature, dense_ctx_t, tables, W1, b1, W2, b2, W3, out):
    batch, FEATS = ids.shape
    D = tables[0].shape[1]
    TILES = batch // P
    CTX = dense_ctx_t.shape[0]
    H1, H2 = W2.shape
    H1C, H2C = H1 // P, H2 // P

    SLOTS = (FEATS - 1 + 1) // QUADS + 1
    MOVED_SLOTS = 3
    K_SLOTS = SLOTS - MOVED_SLOTS
    SHORT = QUADS * MOVED_SLOTS - 2
    GAP = QUAD - SHORT
    assert QUADS * 2 * MOVED_SLOTS - 2 <= GAP
    FIRST_SLOT = [1, 1, 0, 0]
    CTX_AT = QUADS * MOVED_SLOTS - 1
    assert CTX_AT + CTX <= QUAD

    gathered_features = [f for f in range(FEATS) if f not in LOOKED_UP]
    FGROUPS = [gathered_features[n:n + 4] for n in range(0, len(gathered_features), 4)]
    NFG = len(FGROUPS)
    NK = len(LOOKED_UP)
    CH = tables[LOOKED_UP[0]].shape[0] // ROWS_K
    SPRAY = 120
    RING = 3

    DVE_CH = CH - 1

    SG = QUADS
    UNITG = 8
    UNITS = P // (SG * UNITG)
    WIDTH = SG * (FEATS - 1)

    with ExitStack() as ctx:
        def sb(name, shape, dt=F32):
            return ctx.enter_context(nc.sbuf_tensor(name, shape, dt))

        def pb(name, shape):
            return ctx.enter_context(nc.psum_tensor(name, shape, F32))

        def sem(name):
            return ctx.enter_context(nc.semaphore(name))

        ids_sb = sb("ids_sb", [P, TILES, FEATS], I32)
        emb = sb("emb", [P, TILES, sum(map(len, FGROUPS)), D])
        embT = sb("embT", [P, TILES, P, QUAD])
        table = sb("table", [P, RING, CH, D])
        idrow = sb("idrow", [P, RING, batch], I32)
        idrel = sb("idrel", [P, 2, batch])
        hi = sb("hi", [P, 2, CH, D], F32R)
        lo = sb("lo", [P, 2, CH, D], F32R)
        onehot = sb("onehot", [P, 2, CH, batch], F32R)
        base_i = sb("base_i", [P, 1], I32)
        base_f = sb("base_f", [P, 1])
        pairs = sb("pairs", [P, 2, SLOTS, P])
        w1_sb = sb("w1_sb", [P, K_SLOTS, H1])
        w2_sb = sb("w2_sb", [P, H1C, H2])
        w3_sb = sb("w3_sb", [P, H2C])
        b1_sb = sb("b1_sb", [P, H1C])
        b2_sb = sb("b2_sb", [P, H2C])
        h1T = sb("h1T", [P, H1C, P])
        h2T = sb("h2T", [P, H2C, P])
        y_sb = sb("y_sb", [P, TILES])
        ident = sb("ident", [P, P])
        zero = sb("zero", [P, 1])
        chunk = sb("chunk", [P, 1])
        near = sb("near", [P, batch])

        tr_ps = pb("tr_ps", [P, 2, 4, P])
        gram_ps = pb("gram_ps", [P, 2, UNITG, P])
        acc = pb("acc", [P, 2, 4 * P])

        ids_loaded = sem("ids_loaded")
        table_loaded = [sem(f"table_loaded{r}") for r in range(RING)]
        gathered = [sem(f"gathered{g}") for g in range(NFG)]
        w1_zeroed = sem("w1_zeroed")
        zero_ready = sem("zero_ready")
        pads_zeroed = sem("pads_zeroed")
        ident_zero = sem("ident_zero")
        ident_ready = sem("ident_ready")
        base_i_ready = sem("base_i_ready")
        base_f_ready = sem("base_f_ready")
        idrel_ready = sem("idrel_ready")
        near_ready = sem("near_ready")
        chunk_ready = sem("chunk_ready")
        weights_loaded = sem("weights_loaded")
        w1_loaded = sem("w1_loaded")
        onehot_by_dve = sem("onehot_by_dve")
        onehot_by_act = sem("onehot_by_act")
        hi_ready = sem("hi_ready")
        lo_ready = sem("lo_ready")
        looked_up = sem("looked_up")
        vectors_out = sem("vectors_out")
        transposed = sem("transposed")
        embT_by = [sem("embT_by_dve"), sem("embT_by_act")]
        gram_done = sem("gram_done")
        pairs_by_dve = sem("pairs_by_dve")
        pairs_by_act = sem("pairs_by_act")
        rows_moved = sem("rows_moved")
        h1_done = sem("h1_done")
        relu1_by_act = sem("relu1_by_act")
        relu1_by_dve = sem("relu1_by_dve")
        h2_done = sem("h2_done")
        relu2_by_act = sem("relu2_by_act")
        relu2_by_dve = sem("relu2_by_dve")
        y_done = sem("y_done")
        y_copied = sem("y_copied")
        stored = sem("stored")

        def tr(t, groups):
            return [("transposes", t, g) for g in groups] if t < TILES else []

        STEPS = [("gram", 0, u) for u in range(UNITS)]
        for t in range(1, TILES):
            done = 0 if t == 1 else 2
            STEPS += tr(t, range(done, NFG)) + [("gram", t, 0), ("gram", t, 1)]
            if t < TILES - 1:
                STEPS += [("h1", t - 1, None), ("gram", t, 2)] + tr(t + 1, [0])
                STEPS += [("h2", t - 1, None), ("gram", t, 3)] + tr(t + 1, [1]) + [("y", t - 1, None)]
            else:
                STEPS += [("gram", t, 2), ("gram", t, 3)]
                STEPS += [(layer, n, None) for n in (t - 1, t) for layer in ("h1", "h2", "y")]
        MOVES = QUADS + 1

        def tr_index(t, g):
            return t * NFG + g

        block = ctx.enter_context(nc.Block())

        @block.sync
        def _(sp):
            def load_table(k):
                f, r = LOOKED_UP[k], k % RING
                if k >= RING:
                    sp.wait_ge(lo_ready, k - RING + 1)
                src = tables[f].rearrange("(k c) d -> k c d", c=CH)
                sp.dma_start(idrow[0:ROWS_K, r, :],
                             ids_by_feature[f].partition_broadcast(ROWS_K)).then_inc(table_loaded[r], 16)
                sp.dma_start(table[0:SPRAY, r, :, :], src[0:SPRAY, :, :]).then_inc(table_loaded[r], 16)
                sp.dma_start(table[SPRAY:ROWS_K, r, :, :], src[SPRAY:, :, :]).then_inc(table_loaded[r], 16)

            sp.dma_start(ids_sb[:, :, :], ids.rearrange("(p t) f -> p t f", t=TILES)).then_inc(ids_loaded, 16)
            for k in range(RING):
                load_table(k)
            sp.dma_start(b1_sb[:, :], b1).then_inc(weights_loaded, 16)
            sp.dma_start(b2_sb[:, :], b2).then_inc(weights_loaded, 16)
            sp.dma_start(w3_sb[:, :], W3).then_inc(weights_loaded, 16)
            for k in range(RING, NK):
                load_table(k)
            sp.wait_ge(w1_zeroed, 1)
            row = 0
            for j in range(1, FEATS):
                a, q = divmod(j + 1, QUADS)
                at = QUAD * q + (GAP if a < MOVED_SLOTS else 0)
                sp.dma_start(w1_sb[at:at + j, a if a < MOVED_SLOTS else a - MOVED_SLOTS, :],
                             W1[row:row + j, :]).then_inc(w1_loaded, 16)
                row += j
            sp.dma_start(w1_sb[CTX_AT:CTX_AT + CTX, 0, :], W1[row:row + CTX, :]).then_inc(w1_loaded, 16)
            sp.dma_start(w2_sb[:, :, :], W2.rearrange("(c k) n -> k c n", k=P)).then_inc(weights_loaded, 16)
            for t in range(TILES):
                sp.wait_ge(pairs_by_dve, UNITS * (t + 1))
                sp.wait_ge(pairs_by_act, UNITS * (t + 1))
                if t > 0:
                    sp.wait_ge(rows_moved, 16 * MOVES * t)
                for q in range(QUADS):
                    sp.dma_start(pairs[QUAD * q + GAP:QUAD * (q + 1), t % 2, FIRST_SLOT[q] + MOVED_SLOTS:2 * MOVED_SLOTS, :],
                                 pairs[QUAD * q:QUAD * q + SHORT, t % 2, FIRST_SLOT[q]:MOVED_SLOTS, :],
                                 ).then_inc(rows_moved, 16)
                sp.dma_start(pairs[CTX_AT:CTX_AT + CTX, t % 2, MOVED_SLOTS, :],
                             dense_ctx_t[:, t, :]).then_inc(rows_moved, 16)
            sp.wait_ge(y_copied, 1)
            sp.dma_start(out.rearrange("(p t) o -> p (t o)", t=TILES), y_sb[:, :]).then_inc(stored, 16)
            sp.wait_ge(stored, 16)

        @block.gpsimd
        def _(pool):
            nc.gpsimd.iota(base_i[:, :], pattern=[[0, 1]], base=0, channel_multiplier=-CH).then_inc(base_i_ready, 1)
            nc.gpsimd.memset(ident[:, :], 0.0).then_inc(ident_zero, 1)
            pool.wait_ge(ident_zero, 1)
            nc.gpsimd.affine_select(out=ident[:, :], in_=ident[:, :], compare_op=ALU.not_equal, fill=1.0,
                                    base=0, pattern=[[-1, P]], channel_multiplier=1).then_inc(ident_ready, 1)
            pool.wait_ge(ids_loaded, 16)
            for t in range(TILES):
                n = 0
                for g, group in enumerate(FGROUPS):
                    if t > 0:
                        pool.wait_ge(gathered[g], 16 * len(group) * t)
                    for f in group:
                        pool.indirect_dma_start(emb[:, t, n, :], None, tables[f],
                                                bass.IndirectOffsetOnAxis(ids_sb[:, t, f:f + 1], 0),
                                                ).then_inc(gathered[g], 16)
                        n += 1

        @block.tensor
        def _(pe):
            def transposes(t, g):
                n = tr_index(t, g)
                pe.wait_ge(gathered[g], 16 * len(FGROUPS[g]) * (t + 1))
                if n >= 2:
                    pe.wait_ge(embT_by[n % 2], n // 2)
                first = sum(map(len, FGROUPS[:g]))
                for k in range(len(FGROUPS[g])):
                    last = nc.tensor.transpose(tr_ps[:, n % 2, k, :], emb[:, t, first + k, :], ident[:, :])
                last.then_inc(transposed, 1)

            def look_up(k):
                b = k % 2
                pe.wait_ge(hi_ready, k + 1)
                if k >= 2:
                    pe.wait_ge(vectors_out, k - 1)
                for c in range(CH):
                    if c < DVE_CH:
                        pe.wait_ge(onehot_by_dve, DVE_CH * k + c + 1)
                    else:
                        pe.wait_ge(onehot_by_act, k + 1)
                    nc.tensor.matmul(acc[:, b, :], hi[0:ROWS_K, b, c, :], onehot[0:ROWS_K, b, c, :],
                                     start=(c == 0), stop=False)
                pe.wait_ge(lo_ready, k + 1)
                for c in range(CH):
                    last = nc.tensor.matmul(acc[:, b, :], lo[0:ROWS_K, b, c, :], onehot[0:ROWS_K, b, c, :],
                                            start=False, stop=(c == CH - 1))
                last.then_inc(looked_up, 1)

            def gram(t, n):
                if n == 0:
                    groups = tr_index(t + 1, 0)
                    pe.wait_ge(embT_by[0], -(-groups // 2))
                    pe.wait_ge(embT_by[1], groups // 2)
                u = UNITS * t + n
                if u >= 2:
                    pe.wait_ge(pairs_by_dve, u - 1)
                    pe.wait_ge(pairs_by_act, u - 1)
                for g in range(UNITG):
                    p0 = SG * (UNITG * n + g)
                    last = nc.tensor.matmul(gram_ps[:, u % 2, g, 0:WIDTH], embT[:, t, p0:p0 + SG, :],
                                            embT[:, t, p0:p0 + SG, 1:FEATS], start=True, stop=True)
                last.then_inc(gram_done, 1)

            def h1(t):
                pe.wait_ge(pairs_by_dve, UNITS * (t + 1))
                pe.wait_ge(pairs_by_act, UNITS * (t + 1))
                pe.wait_ge(w1_loaded, 16 * FEATS)
                pe.wait_ge(rows_moved, 16 * MOVES * (t + 1))
                for n in range(H1C):
                    for a in range(K_SLOTS):
                        last = nc.tensor.matmul(acc[:, n // 2, P * (n % 2):P * (n % 2 + 1)],
                                                w1_sb[:, a, P * n:P * (n + 1)], pairs[:, t % 2, a + MOVED_SLOTS, :],
                                                start=(a == 0), stop=(a == K_SLOTS - 1))
                    if n % 2 == 1:
                        last.then_inc(h1_done, 1)

            def h2(t):
                pe.wait_ge(weights_loaded, 16 * 4)
                pe.wait_ge(relu1_by_act, t + 1)
                pe.wait_ge(relu1_by_dve, t + 1)
                for m in range(H2C):
                    for c in range(H1C):
                        last = nc.tensor.matmul(acc[:, m, 2 * P:3 * P], w2_sb[:, c, P * m:P * (m + 1)], h1T[:, c, :],
                                                start=(c == 0), stop=(c == H1C - 1))
                    last.then_inc(h2_done, 1)

            def y(t):
                pe.wait_ge(relu2_by_act, t + 1)
                pe.wait_ge(relu2_by_dve, t + 1)
                for m in range(H2C):
                    last = nc.tensor.matmul(acc[:, 1, 3 * P + t:3 * P + t + 1], h2T[:, m, :], w3_sb[:, m:m + 1],
                                            start=(m == 0), stop=(m == H2C - 1))
                last.then_inc(y_done, 1)

            pe.wait_ge(ident_ready, 1)
            for k in range(NK):
                if k >= NK - NFG:
                    transposes(0, k - (NK - NFG))
                look_up(k)
            pe.wait_ge(vectors_out, NK)
            pe.wait_ge(pads_zeroed, 1)
            for kind, t, arg in STEPS:
                if kind == "transposes":
                    transposes(t, arg)
                elif kind == "gram":
                    gram(t, arg)
                elif kind == "h1":
                    h1(t)
                elif kind == "h2":
                    h2(t)
                else:
                    y(t)

        def move_pairs(copy, t, n, s):
            view = gram_ps[QUAD * s:QUAD * (s + 1), (UNITS * t + n) % 2, :, :]
            p0 = SG * UNITG * n
            for q in range(QUADS):
                a = FIRST_SLOT[q]
                col = (FEATS - 1) * s + QUADS * a + q - 2
                src = view[:, :, col:col + QUADS * (SLOTS - 1 - a) + 1:QUADS]
                dst = pairs[QUAD * q:QUAD * (q + 1), t % 2, a:SLOTS, p0 + s:p0 + SG * UNITG:SG]
                last = copy(dst.rearrange("r a g -> r g a"), src)
            return last

        def move_vectors(copy, t, g):
            for k, f, n in runs(FGROUPS[g]):
                last = copy(embT[:, t, :, f:f + n],
                            tr_ps[:, tr_index(t, g) % 2, k:k + n, :].rearrange("d f p -> d p f"))
            return last

        @block.vector
        def _(dve):
            def transposes(t, g):
                if tr_index(t, g) % 2 == 0:
                    dve.wait_ge(transposed, tr_index(t, g) + 1)
                    move_vectors(nc.vector.tensor_copy, t, g).then_inc(embT_by[0], 1)

            nc.vector.memset(zero[:, :], 0.0).then_inc(zero_ready, 1)
            nc.vector.memset(chunk[:, :], -float(CH - 1)).then_inc(chunk_ready, 1)
            dve.wait_ge(base_i_ready, 1)
            nc.vector.tensor_copy(base_f[:, :], base_i[:, :]).then_inc(base_f_ready, 1)
            nc.vector.memset(w1_sb[:, :, :], 0.0).then_inc(w1_zeroed, 1)
            for k in range(NK):
                r, b = k % RING, k % 2
                dve.wait_ge(idrel_ready, k + 1)
                if k >= 2:
                    dve.wait_ge(looked_up, k - 1)
                for c in range(DVE_CH):
                    nc.vector.tensor_scalar(onehot[0:ROWS_K, b, c, :], idrel[0:ROWS_K, b, :], float(c), None,
                                            ALU.is_equal).then_inc(onehot_by_dve, 1)
                dve.wait_ge(hi_ready, k + 1)
                nc.vector.tensor_tensor(lo[0:ROWS_K, b, :, :], table[0:ROWS_K, r, :, :], hi[0:ROWS_K, b, :, :],
                                        ALU.subtract).then_inc(lo_ready, 1)
                if k > NK - NFG:
                    transposes(0, k - 1 - (NK - NFG))
            transposes(0, NFG - 1)
            for kind, t, arg in STEPS:
                if kind == "transposes":
                    transposes(t, arg)
                elif kind == "gram":
                    if t >= 2 and arg == 0:
                        dve.wait_ge(h1_done, 2 * (t - 1))
                    dve.wait_ge(gram_done, UNITS * t + arg + 1)
                    for s in (0, 1):
                        last = move_pairs(nc.vector.tensor_copy, t, arg, s)
                    last.then_inc(pairs_by_dve, 1)
                elif kind == "h1":
                    dve.wait_ge(weights_loaded, 16 * 4)
                    dve.wait_ge(h1_done, 2 * t + 2)
                    for n in (2, 3):
                        last = nc.vector.tensor_scalar(h1T[:, n, :], acc[:, 1, P * (n % 2):P * (n % 2 + 1)],
                                                       b1_sb[:, n:n + 1], 0.0, ALU.add, ALU.max)
                    last.then_inc(relu1_by_dve, 1)
                elif kind == "h2":
                    dve.wait_ge(h2_done, 2 * t + 2)
                    nc.vector.tensor_scalar(h2T[:, 1, :], acc[:, 1, 2 * P:3 * P], b2_sb[:, 1:2], 0.0,
                                            ALU.add, ALU.max).then_inc(relu2_by_dve, 1)
            dve.wait_ge(y_done, TILES)
            nc.vector.tensor_copy(y_sb[:, :], acc[:, 1, 3 * P:3 * P + TILES]).then_inc(y_copied, 1)

        @block.scalar
        def _(act):
            def transposes(t, g):
                if tr_index(t, g) % 2 == 1:
                    act.wait_ge(transposed, tr_index(t, g) + 1)
                    move_vectors(nc.scalar.copy, t, g).then_inc(embT_by[1], 1)

            def vectors(k):
                act.wait_ge(looked_up, k + 1)
                nc.scalar.copy(embT[:, :, :, LOOKED_UP[k]],
                               acc[:, k % 2, :].rearrange("d (t p) -> d t p", t=TILES)).then_inc(vectors_out, 1)

            act.wait_ge(base_f_ready, 1)
            for k in range(NK):
                r, b = k % RING, k % 2
                act.wait_ge(table_loaded[r], 16 * 3 * (k // RING + 1))
                if k >= 2:
                    act.wait_ge(looked_up, k - 1)
                nc.scalar.activation(idrel[0:ROWS_K, b, :], idrow[0:ROWS_K, r, :], ACT.Identity,
                                     bias=base_f[0:ROWS_K, :]).then_inc(idrel_ready, 1)
                nc.scalar.copy(hi[0:ROWS_K, b, :, :], table[0:ROWS_K, r, :, :]).then_inc(hi_ready, 1)
                act.wait_ge(idrel_ready, k + 1)
                act.wait_ge(chunk_ready, 1)
                nc.scalar.activation(near[0:ROWS_K, :], idrel[0:ROWS_K, b, :], ACT.Square,
                                     bias=chunk[0:ROWS_K, :]).then_inc(near_ready, 1)
                act.wait_ge(near_ready, k + 1)
                nc.scalar.activation(onehot[0:ROWS_K, b, CH - 1, :], near[0:ROWS_K, :], ACT.Relu,
                                     bias=1.0, scale=-1.0).then_inc(onehot_by_act, 1)
                if k == 0:
                    act.wait_ge(zero_ready, 1)
                    pads = embT[:, :, :, FEATS:QUAD].rearrange("d t p f -> d (t p) f")
                    nc.scalar.copy(pads, zero[:, :].unsqueeze(2).to_broadcast(list(pads.shape))).then_inc(pads_zeroed, 1)
                if k >= 1:
                    vectors(k - 1)
                if k > NK - NFG:
                    transposes(0, k - 1 - (NK - NFG))
            transposes(0, NFG - 1)
            vectors(NK - 1)
            for kind, t, arg in STEPS:
                if kind == "transposes":
                    transposes(t, arg)
                elif kind == "gram":
                    if t >= 2 and arg == 0:
                        act.wait_ge(h1_done, 2 * (t - 1))
                    act.wait_ge(gram_done, UNITS * t + arg + 1)
                    for s in (2, 3):
                        last = move_pairs(nc.scalar.copy, t, arg, s)
                    last.then_inc(pairs_by_act, 1)
                elif kind == "h1":
                    act.wait_ge(weights_loaded, 16 * 4)
                    act.wait_ge(h1_done, 2 * t + 1)
                    for n in (0, 1):
                        last = nc.scalar.activation(h1T[:, n, :], acc[:, 0, P * n:P * (n + 1)], ACT.Relu,
                                                    bias=b1_sb[:, n:n + 1])
                    last.then_inc(relu1_by_act, 1)
                elif kind == "h2":
                    act.wait_ge(h2_done, 2 * t + 1)
                    nc.scalar.activation(h2T[:, 0, :], acc[:, 0, 2 * P:3 * P], ACT.Relu,
                                         bias=b2_sb[:, 0:1]).then_inc(relu2_by_act, 1)


def kernel(**inputs):
    import numpy as np
    import concourse.bacc as bacc
    from concourse.bass_utils import run_bass_kernel_spmd

    ids, ctx = inputs["ids"], inputs["dense_ctx"]
    tiles = ids.shape[0] // P
    laid = {
        "ids": ids,
        "ids_by_feature": ids.reshape(P, tiles, -1).transpose(2, 1, 0).reshape(-1, ids.shape[0]),
        "ctx_t": ctx.reshape(P, tiles, -1).transpose(2, 1, 0),
        "W1": inputs["W_top1"],
        "b1": inputs["b_top1"].reshape(-1, P).T,
        "W2": inputs["W_top2"],
        "b2": inputs["b_top2"].reshape(-1, P).T,
        "W3": inputs["W_top3"].reshape(-1, P).T,
    }
    feats = ids.shape[1]
    for f in range(feats):
        laid[f"tbl_{f}"] = inputs[f"tbl_{f}"]

    nc = bacc.Bacc("TRN2", target_bir_lowering=False, num_devices=1)
    arrays, aps = {}, {}
    for name, a in laid.items():
        a = np.ascontiguousarray(a)
        arrays[f"in_{name}"] = a
        aps[name] = nc.dram_tensor(f"in_{name}", a.shape, mybir.dt.from_np(a.dtype), kind="ExternalInput").ap()
    out = nc.dram_tensor("out_y", (ids.shape[0], 1), F32, kind="ExternalOutput").ap()
    build_tower(nc, aps["ids"], aps["ids_by_feature"], aps["ctx_t"], [aps[f"tbl_{f}"] for f in range(feats)],
                aps["W1"], aps["b1"], aps["W2"], aps["b2"], aps["W3"], out)
    r = run_bass_kernel_spmd(nc, [arrays], core_ids=[0])
    return r.results[0]["out_y"]
```

```python
from contextlib import ExitStack

import concourse.bass as bass
from concourse import mybir

F32 = mybir.dt.float32
F32R = mybir.dt.float32r
I32 = mybir.dt.int32
ALU = mybir.AluOpType
ACT = mybir.ActivationFunctionType

P = 128
QUAD = 32
QUADS = P // QUAD
LOOKED_UP = [4, 6, 7, 8, 11, 12, 15, 20, 21, 3]
LAST_LOOKED_UP_TILES = 2
ROWS_K = 125


def runs(features):
    out = []
    for n, f in enumerate(features):
        if out and out[-1][1] + out[-1][2] == f:
            out[-1][2] += 1
        else:
            out.append([n, f, 1])
    return out


def build_tower(nc, ids, ids_by_feature, dense_ctx_t, tables, W1, b1, W2, b2, W3, out):
    batch, FEATS = ids.shape
    D = tables[0].shape[1]
    TILES = batch // P
    CTX = dense_ctx_t.shape[0]
    H1, H2 = W2.shape
    H1C, H2C = H1 // P, H2 // P

    SLOTS = (FEATS - 1 + 1) // QUADS + 1
    MOVED_SLOTS = 3
    K_SLOTS = SLOTS - MOVED_SLOTS
    UNMOVED = K_SLOTS - 1
    SHORT = QUADS * MOVED_SLOTS - 2
    GAP = QUAD - SHORT
    assert QUADS * 2 * MOVED_SLOTS - 2 <= GAP
    FIRST_SLOT = [1, 1, 0, 0]
    CTX_ROWS = CTX // 2
    assert CTX_ROWS <= SHORT

    split_feature = LOOKED_UP[-1]
    gathered_features = [f for f in range(FEATS) if f not in LOOKED_UP] + [split_feature]
    FGROUPS = [gathered_features[n:n + 4] for n in range(0, len(gathered_features), 4)]
    NFG = len(FGROUPS)

    def group(t, g):
        return [f for f in FGROUPS[g] if t < TILES - LAST_LOOKED_UP_TILES or f != split_feature]

    def rows_gathered(t, g):
        return 16 * sum(len(group(i, g)) for i in range(t + 1))

    NK = len(LOOKED_UP)
    CHS = [tables[f].shape[0] // ROWS_K for f in LOOKED_UP]
    CH = CHS[0]
    assert CHS[:-1] == [CH] * (NK - 1)
    LTILES = [slice(0, TILES)] * (NK - 1) + [slice(TILES - LAST_LOOKED_UP_TILES, TILES)]
    COLS = [P * (tl.stop - tl.start) for tl in LTILES]
    assert CHS[-1] * COLS[-1] <= CH * COLS[0]
    SPRAY = 120
    RING = 3
    EARLY = 2
    WARM = 10

    DVE_CHS = [ch - 1 for ch in CHS]

    SG = QUADS
    UNITG = 8
    UNITS = P // (SG * UNITG)
    WIDTH = SG * (FEATS - 1)
    ROWS = QUAD * (SG - 1) + FEATS - 1

    with ExitStack() as ctx:
        def sb(name, shape, dt=F32):
            return ctx.enter_context(nc.sbuf_tensor(name, shape, dt))

        def pb(name, shape):
            return ctx.enter_context(nc.psum_tensor(name, shape, F32))

        def sem(name):
            return ctx.enter_context(nc.semaphore(name))

        ids_sb = sb("ids_sb", [P, TILES, FEATS], I32)
        emb = sb("emb", [P, TILES, sum(map(len, FGROUPS)), D])
        embT = sb("embT", [P, TILES, P, QUAD])
        table = sb("table", [P, RING, CHS[-1], D])
        idrow = sb("idrow", [P, RING, batch], I32)
        idrel = sb("idrel", [P, 2, batch])
        hi = sb("hi", [P, 2, CHS[-1], D], F32R)
        lo = sb("lo", [P, 2, CHS[-1], D], F32R)
        onehot = sb("onehot", [P, 2, CH * batch], F32R)
        base_i = sb("base_i", [P, 2], I32)
        base_f = sb("base_f", [P, 2])
        pairs = sb("pairs", [P, 2, SLOTS, P])
        w1_sb = sb("w1_sb", [P, K_SLOTS, H1])
        w2_sb = sb("w2_sb", [P, H1C, H2])
        w3_sb = sb("w3_sb", [P, H2C])
        b1_sb = sb("b1_sb", [P, H1C])
        b2_sb = sb("b2_sb", [P, H2C])
        h1T = sb("h1T", [P, 2, H1C, P])
        h2T = sb("h2T", [P, 2, H2C, P])
        y_sb = sb("y_sb", [P, TILES])
        ident = sb("ident", [P, P])
        blank = sb("blank", [P, P])
        warm = sb("warm", [P, 1])
        chunk = sb("chunk", [P, 2])
        near = sb("near", [P, batch])

        tr_ps = pb("tr_ps", [P, 2, 4, P])
        gram_ps = pb("gram_ps", [P, 2, UNITG, P])
        acc = pb("acc", [P, 2, 4 * P])

        ids_loaded = sem("ids_loaded")
        first_part_loaded = sem("first_part_loaded")
        table_loaded = [sem(f"table_loaded{r}") for r in range(RING)]
        gathered = [sem(f"gathered{g}") for g in range(NFG)]
        w1_zeroed = sem("w1_zeroed")
        pads_zeroed = sem("pads_zeroed")
        blank_ready = sem("blank_ready")
        ident_zero = sem("ident_zero")
        ident_ready = sem("ident_ready")
        base_i_ready = sem("base_i_ready")
        base_f_ready = sem("base_f_ready")
        idrel_ready = sem("idrel_ready")
        near_ready = sem("near_ready")
        chunk_ready = sem("chunk_ready")
        weights_loaded = sem("weights_loaded")
        w1_loaded = sem("w1_loaded")
        onehot_by_dve = sem("onehot_by_dve")
        onehot_by_act = sem("onehot_by_act")
        ids_landed = [sem(f"ids_landed{r}") for r in range(RING)]
        hi_ready = sem("hi_ready")
        lo_ready = sem("lo_ready")
        looked_up = sem("looked_up")
        vectors_out = sem("vectors_out")
        transposed = sem("transposed")
        embT_by = [sem("embT_by_dve"), sem("embT_by_act")]
        gram_done = sem("gram_done")
        pairs_by_dve = sem("pairs_by_dve")
        pairs_by_act = sem("pairs_by_act")
        rows_moved = [sem("rows_moved0"), sem("rows_moved1")]
        pairs_zeroed = sem("pairs_zeroed")
        ctx_loaded = sem("ctx_loaded")
        h1_done = sem("h1_done")
        relu1_by_act = sem("relu1_by_act")
        relu1_by_dve = sem("relu1_by_dve")
        h2_done = sem("h2_done")
        relu2_by_act = sem("relu2_by_act")
        relu2_by_dve = sem("relu2_by_dve")
        y_done = sem("y_done")
        y_copied = sem("y_copied")
        stored = sem("stored")

        def tr(t, groups):
            return [("transposes", t, g) for g in groups] if t < TILES else []

        STEPS = tr(1, range(NK - 2 - NFG, NFG)) + [("gram", 0, n) for n in range(UNITS)]
        for t in range(1, TILES - 1):
            STEPS += [("gram", t, 0), ("gram", t, 1)] + tr(t + 1, [0]) + [("gram", t, 2), ("h1", t - 1, None)]
            STEPS += tr(t + 1, [1, 2]) + [("h2", t - 1, None)]
            STEPS += [("gram half 0", t, 3)] + tr(t + 1, [3]) + [("y", t - 1, None)]
            STEPS += tr(t + 1, [4]) + [("gram half 1", t, 3)]
        t = TILES - 1
        STEPS += [("gram", t, u) for u in range(UNITS)]
        STEPS += [("h1", t - 1, None), ("h1 unmoved slot", t, None), ("h2", t - 1, None), ("h1", t, None),
                  ("y", t - 1, None), ("h2", t, None), ("y", t, None)]
        MOVES = QUADS
        IN_LOOKUPS = [(0, g) for g in range(NFG)] + [(1, g) for g in range(NK - 2 - NFG)]

        def parts(k):
            return [slice(0, CH // 2), slice(CH // 2, CH)] if k < EARLY else [slice(0, CHS[k])]

        def parts_to(k):
            return k + min(k, EARLY)

        def one_hot(k, c):
            return onehot[0:ROWS_K, k % 2, COLS[k] * c:COLS[k] * (c + 1)]

        def own(k):
            return slice(k // (NK - 1), k // (NK - 1) + 1)

        def tr_index(t, g):
            return t * NFG + g

        LAST = TILES - 1

        def h1_ps(t, n):
            return acc[:, n // 2, P * (n % 2):P * (n % 2 + 1)] if t < LAST else gram_ps[:, n // 2, 4 * (n % 2), :]

        def h2_ps(t, m):
            return tr_ps[:, m, 0, :] if t == LAST - 1 else acc[:, m, 2 * P:3 * P]

        def y_ps(t):
            return acc[:, 0, 3 * P + t:3 * P + t + 1] if t < LAST - 1 else gram_ps[:, 0, 0, t:t + 1]

        def h1_read(t, n):
            return H1C * t + (n + 1 if t == LAST else 2 * (n // 2 + 1))

        block = ctx.enter_context(nc.Block())

        @block.sync
        def _(sp):
            def load_table(k):
                f, r = LOOKED_UP[k], k % RING
                if k >= RING:
                    sp.wait_ge(lo_ready, parts_to(k - RING + 1))
                sp.dma_start(idrow[0:ROWS_K, r, :],
                             ids_by_feature[f].partition_broadcast(ROWS_K)).then_inc(ids_landed[r], 16)
                src = tables[f].rearrange("(p c) d -> p c d", c=CHS[k])
                for n, c in enumerate(parts(k) if k == 0 else [slice(0, CHS[k])]):
                    landed = first_part_loaded if k == 0 and n == 0 else table_loaded[r]
                    sp.dma_start(table[0:SPRAY, r, c, :], src[0:SPRAY, c, :]).then_inc(landed, 16)
                    sp.dma_start(table[SPRAY:ROWS_K, r, c, :], src[SPRAY:, c, :]).then_inc(landed, 16)

            sp.dma_start(ids_sb[:, :, :], ids.rearrange("(p t) f -> p t f", t=TILES)).then_inc(ids_loaded, 16)
            for k in range(RING):
                load_table(k)

            def load_context(t):
                for q in range(2):
                    sp.dma_start(pairs[QUAD * q:QUAD * q + CTX_ROWS, t % 2, 0, :],
                                 dense_ctx_t[CTX_ROWS * q:CTX_ROWS * (q + 1), t, :]).then_inc(ctx_loaded, 16)

            sp.dma_start(b1_sb[:, :], b1).then_inc(weights_loaded, 16)
            sp.dma_start(b2_sb[:, :], b2).then_inc(weights_loaded, 16)
            sp.dma_start(w3_sb[:, :], W3).then_inc(weights_loaded, 16)
            for k in range(RING, NK):
                load_table(k)
            sp.wait_ge(w1_zeroed, 1)
            row = 0
            for j in range(1, FEATS):
                a, q = divmod(j + 1, QUADS)
                at = QUAD * q + (GAP if a < MOVED_SLOTS else 0)
                sp.dma_start(w1_sb[at:at + j, a if a < MOVED_SLOTS else a - MOVED_SLOTS, :],
                             W1[row:row + j, :]).then_inc(w1_loaded, 16)
                row += j
            for q in range(2):
                sp.dma_start(w1_sb[QUAD * q + GAP:QUAD * q + GAP + CTX_ROWS, 0, :],
                             W1[row:row + CTX_ROWS, :]).then_inc(w1_loaded, 16)
                row += CTX_ROWS
            sp.dma_start(w2_sb[:, :, :], W2.rearrange("(c k) n -> k c n", k=P)).then_inc(weights_loaded, 16)
            sp.wait_ge(pairs_zeroed, 1)
            load_context(0)
            load_context(1)
            for t in range(TILES):
                sp.wait_ge(pairs_by_dve, UNITS * (t + 1))
                sp.wait_ge(pairs_by_act, UNITS * (t + 1))
                sp.wait_ge(ctx_loaded, 16 * 2 * min(t + 2, TILES))
                for q in range(QUADS):
                    sp.dma_start(pairs[QUAD * q + GAP:QUAD * (q + 1), t % 2, MOVED_SLOTS:2 * MOVED_SLOTS, :],
                                 pairs[QUAD * q:QUAD * q + SHORT, t % 2, 0:MOVED_SLOTS, :]).then_inc(rows_moved[t % 2], 16)
                if t + 2 < TILES:
                    sp.wait_ge(rows_moved[t % 2], 16 * MOVES * (t // 2 + 1))
                    load_context(t + 2)
            sp.wait_ge(y_copied, 2)
            sp.dma_start(out.rearrange("(p t) o -> p (t o)", t=TILES), y_sb[:, :]).then_inc(stored, 16)
            sp.wait_ge(stored, 16)

        @block.gpsimd
        def _(pool):
            for n, ch in enumerate((CH, CHS[-1])):
                nc.gpsimd.iota(base_i[:, n:n + 1], pattern=[[0, 1]], base=0,
                               channel_multiplier=-ch).then_inc(base_i_ready, 1)
            nc.gpsimd.memset(ident[:, :], 0.0).then_inc(ident_zero, 1)
            pool.wait_ge(ident_zero, 1)
            nc.gpsimd.affine_select(out=ident[:, :], in_=ident[:, :], compare_op=ALU.not_equal, fill=1.0,
                                    base=0, pattern=[[-1, P]], channel_multiplier=1).then_inc(ident_ready, 1)
            pool.wait_ge(ids_loaded, 16)
            for t in range(TILES):
                for g in range(NFG):
                    if t > 0:
                        pool.wait_ge(gathered[g], rows_gathered(t - 1, g))
                    for f in group(t, g):
                        pool.indirect_dma_start(emb[:, t, gathered_features.index(f), :], None, tables[f],
                                                bass.IndirectOffsetOnAxis(ids_sb[:, t, f:f + 1], 0),
                                                ).then_inc(gathered[g], 16)

        @block.tensor
        def _(pe):
            def transposes(t, g):
                n = tr_index(t, g)
                pe.wait_ge(gathered[g], rows_gathered(t, g))
                if n >= 2:
                    pe.wait_ge(embT_by[n % 2], n // 2)
                first = sum(map(len, FGROUPS[:g]))
                for k in range(len(group(t, g))):
                    last = nc.tensor.transpose(tr_ps[:, n % 2, k, :], emb[:, t, first + k, :], ident[:, :])
                last.then_inc(transposed, 1)

            def look_up(k):
                b = k % 2
                if k >= 2:
                    pe.wait_ge(vectors_out, k - 1)
                for c in range(CHS[k]):
                    for n, part in enumerate(parts(k)):
                        if c == part.start:
                            pe.wait_ge(hi_ready, parts_to(k) + n + 1)
                    if c < DVE_CHS[k]:
                        pe.wait_ge(onehot_by_dve, sum(DVE_CHS[:k]) + c + 1)
                    else:
                        pe.wait_ge(onehot_by_act, k + 1)
                    nc.tensor.matmul(acc[:, b, 0:COLS[k]], hi[0:ROWS_K, b, c, :], one_hot(k, c),
                                     start=(c == 0), stop=False)
                for c in range(CHS[k]):
                    for n, part in enumerate(parts(k)):
                        if c == part.start:
                            pe.wait_ge(lo_ready, parts_to(k) + n + 1)
                    last = nc.tensor.matmul(acc[:, b, 0:COLS[k]], lo[0:ROWS_K, b, c, :], one_hot(k, c),
                                            start=False, stop=(c == CHS[k] - 1))
                last.then_inc(looked_up, 1)

            def gram(t, n, groups):
                if t == 0 and n == 0:
                    pe.wait_ge(vectors_out, NK)
                    pe.wait_ge(pads_zeroed, 1)
                if n == 0:
                    count = tr_index(t + 1, 0)
                    pe.wait_ge(embT_by[0], -(-count // 2))
                    pe.wait_ge(embT_by[1], count // 2)
                u = UNITS * t + n
                if u >= 2:
                    pe.wait_ge(pairs_by_dve, u - 1)
                    pe.wait_ge(pairs_by_act, u - 1)
                vectors = embT[:, t, :, :].rearrange("d p f -> d (p f)")
                for g in groups:
                    p0 = SG * (UNITG * n + g)
                    last = nc.tensor.matmul(gram_ps[0:ROWS, u % 2, g, 0:WIDTH], vectors[:, QUAD * p0:QUAD * p0 + ROWS],
                                            embT[:, t, p0:p0 + SG, 1:FEATS], start=True, stop=True)
                if g == UNITG - 1:
                    last.then_inc(gram_done, 1)

            def h1(t, slots):
                pe.wait_ge(pairs_by_dve, UNITS * (t + 1))
                pe.wait_ge(pairs_by_act, UNITS * (t + 1))
                pe.wait_ge(w1_loaded, 16 * (FEATS + 1))
                for n in range(H1C):
                    for a in slots:
                        if n == 0 and a == 0:
                            pe.wait_ge(rows_moved[t % 2], 16 * MOVES * (t // 2 + 1))
                        last = nc.tensor.matmul(h1_ps(t, n),
                                                w1_sb[:, a, P * n:P * (n + 1)], pairs[:, t % 2, a + MOVED_SLOTS, :],
                                                start=(a == UNMOVED), stop=(a == UNMOVED - 1))
                    if a == UNMOVED - 1:
                        last.then_inc(h1_done, 1)

            def h2(t):
                pe.wait_ge(weights_loaded, 16 * 4)
                if t == LAST:
                    pe.wait_ge(relu1_by_act, 2 * t)
                    pe.wait_ge(relu1_by_dve, 2 * t)
                if t < LAST - 1:
                    pe.wait_ge(relu1_by_act, 2 * t + 2)
                for m in range(H2C):
                    for c in range(H1C):
                        if m == 0:
                            pe.wait_ge(relu1_by_act if c < 2 else relu1_by_dve, 2 * t + c % 2 + 1)
                        last = nc.tensor.matmul(h2_ps(t, m), w2_sb[:, c, P * m:P * (m + 1)], h1T[:, t % 2, c, :],
                                                start=(c == 0), stop=(c == H1C - 1))
                    last.then_inc(h2_done, 1)

            def y(t):
                if t == LAST - 1:
                    pe.wait_ge(relu1_by_act, 2 * TILES)
                for m in range(H2C):
                    pe.wait_ge((relu2_by_act, relu2_by_dve)[m], t + 1)
                    last = nc.tensor.matmul(y_ps(t), h2T[:, t % 2, m, :], w3_sb[:, m:m + 1],
                                            start=(m == 0), stop=(m == H2C - 1))
                last.then_inc(y_done, 1)

            pe.wait_ge(blank_ready, 1)
            for _ in range(WARM):
                nc.tensor.matmul(tr_ps[:, 1, 0, :], blank[:, :], blank[:, :], start=True, stop=True)
            pe.wait_ge(ident_ready, 1)
            for k in range(NK):
                if k >= 2:
                    transposes(*IN_LOOKUPS[k - 2])
                look_up(k)
            for kind, t, arg in STEPS:
                if kind == "transposes":
                    transposes(t, arg)
                elif kind == "gram":
                    gram(t, arg, range(UNITG))
                elif kind == "gram half 0":
                    gram(t, arg, range(UNITG // 2))
                elif kind == "gram half 1":
                    gram(t, arg, range(UNITG // 2, UNITG))
                elif kind == "h1 unmoved slot":
                    h1(t, [UNMOVED])
                elif kind == "h1":
                    h1(t, range(UNMOVED) if t == LAST else [UNMOVED, *range(UNMOVED)])
                elif kind == "h2":
                    h2(t)
                elif kind == "y":
                    y(t)

        def move_pairs(copy, t, n, s):
            view = gram_ps[QUAD * s:QUAD * s + FEATS - 1, (UNITS * t + n) % 2, :, :]
            p0 = SG * UNITG * n
            for q in range(QUADS):
                a = FIRST_SLOT[q]
                col = (FEATS - 1) * s + QUADS * a + q - 2
                src = view[:, :, col:col + QUADS * (SLOTS - 1 - a) + 1:QUADS]
                dst = pairs[QUAD * q:QUAD * q + FEATS - 1, t % 2, a:SLOTS, p0 + s:p0 + SG * UNITG:SG]
                last = copy(dst.rearrange("r a g -> r g a"), src)
            return last

        def move_vectors(copy, t, g):
            for k, f, n in runs(group(t, g)):
                last = copy(embT[:, t, :, f:f + n],
                            tr_ps[:, tr_index(t, g) % 2, k:k + n, :].rearrange("d f p -> d p f"))
            return last

        @block.vector
        def _(dve):
            def transposes(t, g):
                if tr_index(t, g) % 2 == 0:
                    dve.wait_ge(transposed, tr_index(t, g) + 1)
                    move_vectors(nc.vector.tensor_copy, t, g).then_inc(embT_by[0], 1)

            nc.vector.memset(blank[:, :], 0.0).then_inc(blank_ready, 1)
            for n, ch in enumerate((CH, CHS[-1])):
                nc.vector.memset(chunk[:, n:n + 1], -float(ch - 1)).then_inc(chunk_ready, 1)
            dve.wait_ge(base_i_ready, 2)
            nc.vector.tensor_copy(base_f[:, :], base_i[:, :]).then_inc(base_f_ready, 1)
            nc.vector.memset(pairs[:, :, 0, :], 0.0)
            nc.vector.memset(pairs[:, :, SLOTS - 1, :], 0.0).then_inc(pairs_zeroed, 1)
            nc.vector.memset(embT[:, :, :, FEATS:QUAD], 0.0).then_inc(pads_zeroed, 1)
            for k in range(NK):
                r, b = k % RING, k % 2
                dve.wait_ge(idrel_ready, k + 1)
                if k >= 2:
                    dve.wait_ge(looked_up, k - 1)
                for c in range(DVE_CHS[k]):
                    nc.vector.tensor_scalar(one_hot(k, c), idrel[0:ROWS_K, b, 0:COLS[k]], float(c), None,
                                            ALU.is_equal).then_inc(onehot_by_dve, 1)
                for n, c in enumerate(parts(k)):
                    dve.wait_ge(hi_ready, parts_to(k) + n + 1)
                    nc.vector.tensor_tensor(lo[0:ROWS_K, b, c, :], table[0:ROWS_K, r, c, :], hi[0:ROWS_K, b, c, :],
                                            ALU.subtract).then_inc(lo_ready, 1)
                if k >= 3:
                    transposes(*IN_LOOKUPS[k - 3])
            transposes(*IN_LOOKUPS[NK - 3])
            for kind, t, arg in STEPS:
                if kind == "transposes":
                    transposes(t, arg)
                elif kind in ("gram", "gram half 1"):
                    if t >= 2 and arg == 0:
                        dve.wait_ge(h1_done, H1C * (t - 1))
                    dve.wait_ge(gram_done, UNITS * t + arg + 1)
                    for s in (0, 1):
                        last = move_pairs(nc.vector.tensor_copy, t, arg, s)
                    last.then_inc(pairs_by_dve, 1)
                elif kind == "h1":
                    dve.wait_ge(weights_loaded, 16 * 4)
                    for n in (2, 3):
                        dve.wait_ge(h1_done, h1_read(t, n))
                        nc.vector.tensor_scalar(h1T[:, t % 2, n, :], h1_ps(t, n), b1_sb[:, n:n + 1], 0.0,
                                                ALU.add, ALU.max).then_inc(relu1_by_dve, 1)
                elif kind == "h2":
                    dve.wait_ge(h2_done, 2 * t + 2)
                    nc.vector.tensor_scalar(h2T[:, t % 2, 1, :], h2_ps(t, 1), b2_sb[:, 1:2], 0.0,
                                            ALU.add, ALU.max).then_inc(relu2_by_dve, 1)
            dve.wait_ge(y_done, TILES)
            nc.vector.tensor_copy(y_sb[:, LAST - 1:TILES], gram_ps[:, 0, 0, LAST - 1:TILES]).then_inc(y_copied, 1)

        @block.scalar
        def _(act):
            def transposes(t, g):
                if tr_index(t, g) % 2 == 1:
                    act.wait_ge(transposed, tr_index(t, g) + 1)
                    move_vectors(nc.scalar.copy, t, g).then_inc(embT_by[1], 1)

            def vectors(k):
                act.wait_ge(looked_up, k + 1)
                nc.scalar.copy(embT[:, LTILES[k], :, LOOKED_UP[k]],
                               acc[:, k % 2, 0:COLS[k]].rearrange("d (t p) -> d t p", p=P)).then_inc(vectors_out, 1)

            act.wait_ge(chunk_ready, 2)
            nc.scalar.activation(warm[:, :], chunk[:, 0:1], ACT.Square)
            act.wait_ge(blank_ready, 1)
            nc.scalar.copy(w1_sb.rearrange("p a (n c) -> p (a n) c", c=P),
                           blank[:, :].unsqueeze(1).broadcast_to([P, K_SLOTS * H1C, P])).then_inc(w1_zeroed, 1)
            act.wait_ge(base_f_ready, 1)
            for k in range(NK):
                r, b = k % RING, k % 2
                act.wait_ge(ids_landed[r], 16 * (k // RING + 1))
                if k >= 2:
                    act.wait_ge(looked_up, k - 1)
                nc.scalar.activation(idrel[0:ROWS_K, b, 0:COLS[k]], idrow[0:ROWS_K, r, batch - COLS[k]:batch],
                                     ACT.Identity, bias=base_f[0:ROWS_K, own(k)]).then_inc(idrel_ready, 1)
                for n, c in enumerate(parts(k)):
                    if k == 0 and n == 0:
                        act.wait_ge(first_part_loaded, 16 * 2)
                    else:
                        act.wait_ge(table_loaded[r], 16 * 2 * (k // RING + 1))
                    nc.scalar.copy(hi[0:ROWS_K, b, c, :], table[0:ROWS_K, r, c, :]).then_inc(hi_ready, 1)
                act.wait_ge(idrel_ready, k + 1)
                nc.scalar.activation(near[0:ROWS_K, 0:COLS[k]], idrel[0:ROWS_K, b, 0:COLS[k]], ACT.Square,
                                     bias=chunk[0:ROWS_K, own(k)]).then_inc(near_ready, 1)
                act.wait_ge(near_ready, k + 1)
                nc.scalar.activation(one_hot(k, CHS[k] - 1), near[0:ROWS_K, 0:COLS[k]], ACT.Relu,
                                     bias=1.0, scale=-1.0).then_inc(onehot_by_act, 1)
                if k >= 1:
                    vectors(k - 1)
                if k >= 3:
                    transposes(*IN_LOOKUPS[k - 3])
            transposes(*IN_LOOKUPS[NK - 3])
            vectors(NK - 1)
            for kind, t, arg in STEPS:
                if kind == "transposes":
                    transposes(t, arg)
                elif kind in ("gram", "gram half 1"):
                    if t >= 2 and arg == 0:
                        act.wait_ge(h1_done, H1C * (t - 1))
                    act.wait_ge(gram_done, UNITS * t + arg + 1)
                    for s in (2, 3):
                        last = move_pairs(nc.scalar.copy, t, arg, s)
                    last.then_inc(pairs_by_act, 1)
                elif kind == "h1":
                    act.wait_ge(weights_loaded, 16 * 4)
                    for n in (0, 1):
                        act.wait_ge(h1_done, h1_read(t, n))
                        nc.scalar.activation(h1T[:, t % 2, n, :], h1_ps(t, n), ACT.Relu,
                                             bias=b1_sb[:, n:n + 1]).then_inc(relu1_by_act, 1)
                elif kind == "h2":
                    act.wait_ge(h2_done, 2 * t + 1)
                    nc.scalar.activation(h2T[:, t % 2, 0, :], h2_ps(t, 0), ACT.Relu,
                                         bias=b2_sb[:, 0:1]).then_inc(relu2_by_act, 1)
            act.wait_ge(y_done, LAST - 1)
            nc.scalar.copy(y_sb[:, 0:LAST - 1], acc[:, 0, 3 * P:3 * P + LAST - 1]).then_inc(y_copied, 1)


def kernel(**inputs):
    import numpy as np
    import concourse.bacc as bacc
    from concourse.bass_utils import run_bass_kernel_spmd

    ids, ctx = inputs["ids"], inputs["dense_ctx"]
    tiles = ids.shape[0] // P
    laid = {
        "ids": ids,
        "ids_by_feature": ids.reshape(P, tiles, -1).transpose(2, 1, 0).reshape(-1, ids.shape[0]),
        "ctx_t": ctx.reshape(P, tiles, -1).transpose(2, 1, 0),
        "W1": inputs["W_top1"],
        "b1": inputs["b_top1"].reshape(-1, P).T,
        "W2": inputs["W_top2"],
        "b2": inputs["b_top2"].reshape(-1, P).T,
        "W3": inputs["W_top3"].reshape(-1, P).T,
    }
    feats = ids.shape[1]
    for f in range(feats):
        laid[f"tbl_{f}"] = inputs[f"tbl_{f}"]

    nc = bacc.Bacc("TRN2", target_bir_lowering=False, num_devices=1)
    arrays, aps = {}, {}
    for name, a in laid.items():
        a = np.ascontiguousarray(a)
        arrays[f"in_{name}"] = a
        aps[name] = nc.dram_tensor(f"in_{name}", a.shape, mybir.dt.from_np(a.dtype), kind="ExternalInput").ap()
    out = nc.dram_tensor("out_y", (ids.shape[0], 1), F32, kind="ExternalOutput").ap()
    build_tower(nc, aps["ids"], aps["ids_by_feature"], aps["ctx_t"], [aps[f"tbl_{f}"] for f in range(feats)],
                aps["W1"], aps["b1"], aps["W2"], aps["b2"], aps["W3"], out)
    r = run_bass_kernel_spmd(nc, [arrays], core_ids=[0])
    return r.results[0]["out_y"]
```
